# Optimizing a Trainium2 kernel written in Bass

```python
import numpy as np
import jax
import jax.numpy as jnp

def _softmax(x, axis=-1):
    return jax.nn.softmax(x, axis=axis)

def _gelu(x):
    return jax.nn.gelu(x, approximate=True)

def _silu(x):
    return jax.nn.silu(x)

def _sigmoid(x):
    return jax.nn.sigmoid(x)

def _layernorm(x, axis=-1, eps=1e-05):
    m = jnp.mean(x, axis=axis, keepdims=True)
    v = jnp.var(x, axis=axis, keepdims=True)
    return (x - m) / jnp.sqrt(v + eps)

def _scatter_add(tgt, idx, src, axis=0):
    return tgt.at[idx].add(src)

def _segment_sum(src, seg, n):
    return jax.ops.segment_sum(src, seg, n)
kernel_name = 'mk_cond_resid_d2_seqx_r4_108ae1'

def setup_inputs(seed: int=0):
    np.random.seed(seed)
    _w = jnp.asarray

    def _rec_inputs():
        import jax
        import jax.numpy as jnp
        _rk = jax.random.key(seed)
        x = 7.22e-05 + 1 * jax.random.normal(jax.random.fold_in(_rk, 1), (8, 256, 1024), jnp.float32)
        _lenS = 256 - jax.random.randint(jax.random.fold_in(_rk, 7), (8,), 0, max(1, 256 // 4) + 1, jnp.int32)
        _lenS2 = 256 - jax.random.randint(jax.random.fold_in(_rk, 8), (8,), 0, max(1, 256 // 4) + 1, jnp.int32)
        condB_coeff = 0.00219231 + 0.0100837 * jax.random.normal(jax.random.fold_in(_rk, 11), (8,), jnp.float32)
        itok_B_6_15 = jax.random.randint(jax.random.fold_in(_rk, 13), (8,), 6, 16, jnp.int32)
        _validS = jnp.arange(256)[None, :] < _lenS[:, None]
        _validS2 = jnp.arange(256)[None, :] < _lenS2[:, None]
        _causal = jnp.tril(jnp.ones((256, 256), dtype=bool))
        mask_Bx4096x4096_ik1 = jnp.where(jnp.ones((8, 1024, 1024), dtype=bool), 1, 0).astype(jnp.int32)
        return (x, condB_coeff, itok_B_6_15, mask_Bx4096x4096_ik1)
    x, condB_coeff, itok_B_6_15, mask_Bx4096x4096_ik1 = _rec_inputs()

    def _L0_cond_setup():
        import jax, jax.numpy as jnp
        import numpy as np
        B, S, D_IN, D_OUT = (4, 128, 1024, 1024)
        key = jax.random.key(seed)
        k1, k2, k3, k4, k5 = jax.random.split(key, 5)
        hidden_states = jax.random.normal(k1, (B, S, D_IN), dtype=jnp.float32)
        W = jax.random.normal(k2, (D_OUT, D_IN), dtype=jnp.float32) * 0.02
        b = jax.random.normal(k3, (D_OUT,), dtype=jnp.float32) * 0.02
        coeff = jax.random.normal(k4, (B,), dtype=jnp.float32) * 0.01
        mask = jax.random.randint(k5, (B, D_IN, D_OUT), 0, 2, dtype=jnp.int32)
        return {'hidden_states': hidden_states, 'W': W, 'b': b, 'coeff': coeff, 'mask': mask}
    _L0_cond_all = _L0_cond_setup()
    _L0_cond_in = {k: v for k, v in _L0_cond_all.items() if k in ('W', 'b')}
    del _L0_cond_all

    def _L1_cond_setup():
        import jax, jax.numpy as jnp
        import numpy as np
        B, S, D_IN, D_OUT = (4, 512, 1024, 1024)
        RANK, MAX_LORAS = (16, 32)
        key = jax.random.key(seed)
        ks = jax.random.split(key, 6)
        x = jax.random.normal(ks[0], (B, S, D_IN), dtype=jnp.float32)
        adapter_ids = jax.random.randint(ks[1], (B,), 0, MAX_LORAS)
        base_weight = jax.random.normal(ks[2], (D_OUT, D_IN), dtype=jnp.float32) * D_IN ** (-0.5)
        base_bias = jax.random.normal(ks[3], (D_OUT,), dtype=jnp.float32) * 0.01
        lora_A_w = jax.random.normal(ks[4], (MAX_LORAS, RANK, D_IN), dtype=jnp.float32) * D_IN ** (-0.5)
        lora_B_w = jax.random.normal(ks[5], (MAX_LORAS, D_OUT, RANK), dtype=jnp.float32) * RANK ** (-0.5)
        return {'x': x, 'adapter_ids': adapter_ids, 'base_weight': base_weight, 'base_bias': base_bias, 'lora_A_w': lora_A_w, 'lora_B_w': lora_B_w}
    _L1_cond_all = _L1_cond_setup()
    _L1_cond_in = {k: v for k, v in _L1_cond_all.items() if k in ('base_weight', 'base_bias', 'lora_A_w', 'lora_B_w')}
    del _L1_cond_all
    return {'x': x, 'condB_coeff': condB_coeff, 'itok_B_6_15': itok_B_6_15, 'mask_Bx4096x4096_ik1': mask_Bx4096x4096_ik1, 'L0_cond_W': _L0_cond_in['W'], 'L0_cond_b': _L0_cond_in['b'], 'L1_cond_base_weight': _L1_cond_in['base_weight'], 'L1_cond_base_bias': _L1_cond_in['base_bias'], 'L1_cond_lora_A_w': _L1_cond_in['lora_A_w'], 'L1_cond_lora_B_w': _L1_cond_in['lora_B_w']}

def reference(x, condB_coeff, itok_B_6_15, mask_Bx4096x4096_ik1, L0_cond_W, L0_cond_b, L1_cond_base_weight, L1_cond_base_bias, L1_cond_lora_A_w, L1_cond_lora_B_w):
    import jax
    import jax.numpy as jnp

    def _L0_cond_ref(hidden_states, W, b, coeff, mask):
        import jax, jax.numpy as jnp
        import numpy as np
        B, S, D_IN, D_OUT = (4, 128, 1024, 1024)
        output = jnp.einsum('bsi,oi->bso', hidden_states, W) + b
        sign = (2 * mask - 1).astype(hidden_states.dtype)
        diff = jnp.einsum('bsi,bio->bso', hidden_states, sign)
        return output + diff * coeff[:, None, None]

    def _L1_cond_ref(x, adapter_ids, base_weight, base_bias, lora_A_w, lora_B_w):
        import jax, jax.numpy as jnp
        import numpy as np
        B, S, D_IN, D_OUT = (4, 512, 1024, 1024)
        RANK, MAX_LORAS = (16, 32)
        result = jnp.einsum('bsd,od->bso', x, base_weight) + base_bias
        A = lora_A_w[adapter_ids]
        Bw = lora_B_w[adapter_ids]
        h = jnp.einsum('bsd,brd->bsr', x, A)
        lora_out = jnp.einsum('bsr,bor->bso', h, Bw)
        result = result + lora_out
        return result.astype(x.dtype)
    x = x + _L0_cond_ref(x, L0_cond_W, L0_cond_b, condB_coeff, mask_Bx4096x4096_ik1)
    x = x + _L1_cond_ref(x, itok_B_6_15, L1_cond_base_weight, L1_cond_base_bias, L1_cond_lora_A_w, L1_cond_lora_B_w)
    return x

_drawn_inputs = setup_inputs


def setup_inputs(seed=0):
    import zlib

    import numpy as np

    out = dict(_drawn_inputs(seed))
    spreads = {}
    factors = {'L0_cond_b': 3.499, 'L1_cond_base_bias': 8.0}
    for name, (base, spread) in spreads.items():
        noise = np.random.default_rng([zlib.crc32(name.encode()), seed]).standard_normal(out[name].shape)
        drawn = base * np.exp(spread * noise) if base else spread * noise
        out[name] = jnp.asarray(drawn.astype(out[name].dtype))
    for name, factor in factors.items():
        out[name] = (out[name] * factor).astype(out[name].dtype)
    return out
```

```python
from contextlib import ExitStack

import concourse.bass as bass
from concourse import mybir

F32 = mybir.dt.float32
F32R = mybir.dt.float32r
I32 = mybir.dt.int32
ALU = mybir.AluOpType
ACT = mybir.ActivationFunctionType
AX_X = mybir.AxisListType.X

P = 128
Q = 32
HALF = 512


def two_layer_kernel(nc, x, coeff, ids, mask, W0, b0, W1, b1, lora_a, lora_b, out):
    NB, S, D = x.shape
    NL, R, _ = lora_a.shape
    KT = D // P
    ST = S // P
    OH = D // HALF
    KG = D // HALF
    TG = HALF // P
    SLOTS = 5
    WS = 4
    assert (NB, S, D, R) == (8, 256, 1024, 16) and NB * R == P
    last = NB - 1

    pieces = [("w0", 0, p) for p in range(4)] + [("x", 0)]
    for j in range(4):
        pieces += [("m", j), ("w0", 1, j)]
    pieces += [("x", 1)]
    for j in range(4):
        pieces += [("m", 4 + j), ("w1", 0, j)]
    pieces += [("a",), ("b",), ("b1",)] + [("w1", 1, p) for p in range(4)]
    LEAD = len(pieces)
    batch_pieces = [("m", 0), ("m", 1), ("x", 0), ("m", 2), ("m", 3),
                    ("m", 4), ("m", 5), ("x", 1), ("m", 6), ("m", 7)]
    PER = len(batch_pieces)
    assert PER % SLOTS == 0
    WEIGHT = {"x": 64, "m": 16, "w0": 16, "w1": 16, "a": 16 * NB, "b": 16 * NB, "b1": 16}

    place, filled = {}, [0] * SLOTS
    for n, piece in enumerate(pieces):
        filled[n % SLOTS] += WEIGHT[piece[0]]
        place[piece] = (n % SLOTS, filled[n % SLOTS])

    def slot_of(j):
        return (LEAD + j) % SLOTS

    gain = [sum(WEIGHT[batch_pieces[j][0]] for j in range(PER) if slot_of(j) == s) for s in range(SLOTS)]

    def landed_at(b, piece):
        if isinstance(b, int) and b == 0:
            return place[piece]
        j = batch_pieces.index(piece)
        s = slot_of(j)
        upto = sum(WEIGHT[batch_pieces[i][0]] for i in range(j + 1) if slot_of(i) == s)
        return s, (b - 1) * gain[s] + filled[s] + upto

    units = []
    for p in range(4):
        units += [("w0", 0, p, h) for h in range(2)]
    for j in range(4):
        units += [("w0", 1, j, h) for h in range(2)]
    for j in range(4):
        units += [("w1", 0, j, h) for h in range(2)]
    units += [("a", 0), ("a", 1), ("b", 0), ("b", 1)]
    for p in range(4):
        units += [("w1", 1, p, h) for h in range(2)]
    number = {u: n for n, u in enumerate(units)}
    W0_UNITS = sum(u[0] == "w0" for u in units)

    scratch_a = nc.dram_tensor("adapter_a_parts", [NB, P, KT * 2 * R], F32).ap()
    scratch_b = nc.dram_tensor("adapter_b_parts", [2, P, D], F32).ap()

    with ExitStack() as ctx:
        def sb(name, shape, dt=F32):
            return ctx.enter_context(nc.sbuf_tensor(name, shape, dt))

        def sem(name):
            return ctx.enter_context(nc.semaphore(name))

        load = sb("load", [P, SLOTS, D])
        w0t = sb("w0t", [P, KT, D])
        w1hi = sb("w1hi", [P, KT, D], F32R)
        w1lo = sb("w1lo", [P, KT, D], F32R)
        whi = sb("whi", [P, WS, D], F32R)
        wlo = sb("wlo", [P, WS, D], F32R)
        xt = sb("xt", [P, TG, S])
        xhi = sb("xhi", [P, KT, S], F32R)
        xlo = sb("xlo", [P, KT, S], F32R)
        xy = sb("xy", [P, 2, ST, D])
        yhi = sb("yhi", [P, ST, KT, P], F32R)
        ylo = sb("ylo", [P, ST, KT, P], F32R)
        bias0 = sb("bias0", [P, D])
        bias1lo = sb("bias1lo", [P, D], F32R)
        cs = sb("cs", [P, NB])
        id_row = sb("id_row", [1, NB], I32)
        ident = sb("ident", [P, P])
        at = sb("at", [P, 2, KT, 2 * R], F32R)
        bt = sb("bt", [P, 2, D], F32R)
        hsum = sb("hsum", [P, ST, R])
        ht = sb("ht", [P, S], F32R)
        a_stage = yhi[:, :, :, :].rearrange("p s k m -> p (s k m)").rearrange("p (b k r) -> p b k r", b=NB, k=KT)
        b_stage = ylo[:, :, :, :].rearrange("p s k m -> p (s k m)").rearrange("p (h o) -> p h o", h=2)

        b_sorted_view = xt[:, :, :].rearrange("p t m -> p (t m)")

        ps = ctx.enter_context(nc.psum_tensor("ps", [P, 8, HALF], F32))
        ACC, ZB, TR, SM = 0, 4, 6, 7
        HT0 = 128
        unit_bank = [ZB + u % 3 if u <= number[("b", 1)] else ZB + u % 2 for u in range(len(units))]

        landed = [sem(f"landed{s}") for s in range(SLOTS)]
        ids_in = sem("ids_in")
        coeff_in = sem("coeff_in")
        bias0_in = sem("bias0_in")
        x_in = sem("x_in")
        parts_stored = sem("parts_stored")
        bias1_moved = sem("bias1_moved")
        at_in = sem("at_in")
        bt_in = sem("bt_in")
        z_stored = sem("z_stored")
        ident_set = sem("ident_set")
        zeros_set = sem("zeros_set")
        ones_set = sem("ones_set")
        xb_added = sem("xb_added")
        unit_turned = sem("unit_turned")
        w0_copied = sem("w0_copied")
        parts_hi = sem("parts_hi")
        parts_lo = sem("parts_lo")
        b_sorted = sem("b_sorted")
        bias1_hi = sem("bias1_hi")
        bias1_lo = sem("bias1_lo")
        x_turned = sem("x_turned")
        x_hi = sem("x_hi")
        x_lo = sem("x_lo")
        sign_made = sem("sign_made")
        w_made = sem("w_made")
        w_hi = sem("w_hi")
        w_lo = sem("w_lo")
        w_used = sem("w_used")
        acc_done = sem("acc_done")
        y_made = sem("y_made")
        y_turned = sem("y_turned")
        y_hi = sem("y_hi")
        y_lo = sem("y_lo")
        h_done = sem("h_done")
        h_summed = sem("h_summed")
        h_turned = sem("h_turned")
        h_hi = sem("h_hi")
        h_lo = sem("h_lo")
        z_done = sem("z_done")
        z_made = sem("z_made")

        block = ctx.enter_context(nc.Block())

        def arrived(eng, b, piece):
            s, v = landed_at(b, piece)
            eng.wait_ge(landed[s], v)
            return s

        def split_count(u):
            return u + 1 - min(u + 1, W0_UNITS)

        def split_views(u, part):
            kind = units[u][0]
            bank = ps[:, unit_bank[u], :]
            if kind == "w1":
                _, g, p, h = units[u]
                k0 = g * TG + 2 * h
                w = (w1hi, w1lo)[part]
                return w[:, k0:k0 + 2, 2 * P * p:2 * P * (p + 1)], bank.rearrange("p (k o) -> p k o", k=2)
            h = units[u][1]
            if kind == "a":
                dst = a_stage[:, :, 4 * h:4 * h + 4, part * R:(part + 1) * R].rearrange("p b k r -> p k b r")
                return dst, bank.rearrange("p (k b r) -> p k b r", k=4, b=NB)
            dst = b_stage[:, part, :].rearrange("p (m o) -> p o m", o=8)[:, 4 * h:4 * h + 4, :]
            return dst, bank.rearrange("p (o m) -> p o m", o=4)

        @block.sync
        def _(sp):
            names = []

            def start(s, b, piece):
                kind = piece[0]
                if kind == "x":
                    for a in range(4):
                        c0 = piece[1] * HALF + a * P
                        src = x[bass.ds(b, 1), :, c0:c0 + P].rearrange("e (n q) f -> (e q) n f", q=Q)
                        dst = load[a * Q:(a + 1) * Q, s, :].rearrange("q (n f) -> q n f", f=P)
                        sp.dma_start(dst, src).then_inc(landed[s], 16)
                elif kind == "m":
                    g, t = piece[1] // TG, piece[1] % TG
                    src = mask[bass.ds(b, 1)].rearrange("e (g j t) o -> (e g) t j o", g=KG, t=TG)[g, t]
                    sp.dma_start(load[:, s, :].bitcast(I32), src).then_inc(landed[s], 16)
                elif kind in ("w0", "w1"):
                    w = W0 if kind == "w0" else W1
                    _, g, p = piece
                    src = w[2 * P * p:2 * P * (p + 1), g * HALF:(g + 1) * HALF].rearrange("(t q) f -> q t f", q=P)
                    sp.dma_start(load[:, s, :].rearrange("p (t f) -> p t f", t=2), src).then_inc(landed[s], 16)
                elif kind == "a":
                    for e in range(NB):
                        src = lora_a[bass.ds(names[e], 1)].rearrange("e r d -> (e r) d")
                        sp.dma_start(load[e * R:(e + 1) * R, s, :], src).then_inc(landed[s], 16)
                elif kind == "b":
                    for e in range(NB):
                        src = lora_b[bass.ds(names[e], 1)].rearrange("e (p o) r -> (e p) (o r)", p=P)
                        sp.dma_start(load[:, s, e * P:(e + 1) * P], src).then_inc(landed[s], 16)
                else:
                    sp.dma_start(load[96:97, s, :], b1.rearrange("(e o) -> e o", e=1)).then_inc(landed[s], 16)

            def slot_free(b, piece):
                kind = piece[0]
                if kind == "x":
                    sp.wait_ge(x_turned, 2 * b + piece[1] + 1)
                elif kind == "m":
                    sp.wait_ge(w_lo, KT * b + piece[1] + 1)
                elif kind == "b1":
                    sp.wait_ge(bias1_lo, 1)
                elif kind == "b":
                    sp.wait_ge(b_sorted, 1)
                else:
                    sp.wait_ge(unit_turned, number[(*piece, 1)] + 1)

            def start_batch_piece(b, j, first):
                if j >= SLOTS:
                    slot_free(b, batch_pieces[j - SLOTS])
                elif first:
                    slot_free(0, pieces[LEAD + j - SLOTS])
                else:
                    slot_free(b - 1, batch_pieces[PER + j - SLOTS])
                start(slot_of(j), b, batch_pieces[j])

            def load_rows(b, p, wait):
                if wait:
                    sp.wait_ge(z_stored, 64 * (b - 1))
                src = x[bass.ds(b, 1)].rearrange("e (t q) d -> (e q) t d", q=P)
                sp.dma_start(xy[:, p], src).then_inc(x_in, 16)

            def load_adapter(b, p, wait):
                if wait:
                    sp.wait_ge(z_done, 4 * (b - 1))
                src = scratch_a[bass.ds(b, 1)].rearrange("e p f -> (e p) f")
                sp.dma_start(at[:, p].rearrange("p k r -> p (k r)").bitcast(F32), src).then_inc(at_in, 16)
                for row, part in ((0, 0), (32, 0), (64, 1)):
                    src = scratch_b[part, bass.ds(b * R, R), :]
                    sp.dma_start(bt[row:row + R, p, :].bitcast(F32), src).then_inc(bt_in, 16)

            def store_z(b, p, st, oh):
                sp.wait_ge(z_made, 4 * b + 2 * st + oh + 1)
                dst = out[bass.ds(b, 1), st * P:(st + 1) * P, oh * HALF:(oh + 1) * HALF].rearrange("e q o -> (e q) o")
                sp.dma_start(dst, xy[:, p, st, oh * HALF:(oh + 1) * HALF]).then_inc(z_stored, 16)

            def step(b, p, first=False, end=False):
                q = 1 - p
                if not end:
                    for j in (0, 1, 2, 3, 4, 7, 5, 6, 8) if first else (2, 0, 1, 3, 7, 4, 5, 6, 8):
                        start_batch_piece(b + 1, j, first)
                if not first:
                    store_z(b - 1, q, 1, 0)
                if not end:
                    start_batch_piece(b + 1, 9, first)
                if not first:
                    store_z(b - 1, q, 1, 1)
                if not end:
                    load_rows(b + 1, q, not first)
                    load_adapter(b + 1, q, not first)
                store_z(b, p, 0, 0)
                store_z(b, p, 0, 1)

            sp.dma_start(id_row[:, :], ids.rearrange("(e b) -> e b", e=1)).then_inc(ids_in, 16)
            for n, piece in enumerate(pieces):
                if n >= SLOTS:
                    slot_free(0, pieces[n - SLOTS])
                if n == 5:
                    sp.dma_start(cs[:, :], coeff.rearrange("(e b) -> e b", e=1).to_broadcast([P, NB])).then_inc(coeff_in, 16)
                if piece == ("a",):
                    sp.wait_ge(ids_in, 16)
                    for e in range(NB):
                        names.append(sp.value_load(id_row[0:1, e:e + 1], min_val=0, max_val=NL - 1))
                start(n % SLOTS, 0, piece)
                if piece == ("m", 4):
                    sp.dma_start(bias0[:, :], b0.rearrange("(e o) -> e o", e=1).to_broadcast([P, D])).then_inc(bias0_in, 16)
                    load_rows(0, 0, False)
            sp.wait_ge(parts_lo, split_count(number[("b", 1)]))
            sp.dma_start(scratch_a.rearrange("b p f -> p b f"), a_stage.rearrange("p b k r -> p b (k r)").bitcast(F32)).then_inc(parts_stored, 16)
            sp.dma_start(scratch_b.rearrange("h p o -> p h o"), b_stage.bitcast(F32)).then_inc(parts_stored, 16)
            sp.wait_ge(bias1_lo, 1)
            sp.wait_ge(zeros_set, 1)
            sp.wait_ge(bias1_hi, 2)
            for p in range(2):
                sp.dma_start(bt[97:98, p, :].bitcast(F32), bias1lo[96:97, :].bitcast(F32)).then_inc(bias1_moved, 16)
            sp.wait_ge(parts_stored, 32)
            load_adapter(0, 0, False)
            step(0, 0, first=True)
            with sp.Fori(0, (NB - 2) // 2) as i:
                step(2 * i + 1, 1)
                step(2 * i + 2, 0)
            step(last, 1, end=True)
            store_z(last, 1, 1, 0)
            store_z(last, 1, 1, 1)
            sp.wait_ge(z_stored, 64 * NB)

        @block.gpsimd
        def _(pool):
            nc.gpsimd.memset(ident[:, :], 0.0).then_inc(ident_set, 1)
            pool.wait_ge(ident_set, 1)
            nc.gpsimd.affine_select(out=ident[:, :], in_=ident[:, :], compare_op=ALU.not_equal, fill=1.0, base=0,
                                    pattern=[[-1, P]], channel_multiplier=1).then_inc(ident_set, 1)
            pool.wait_ge(ident_set, 2)
            nc.gpsimd.memset(bt[:, :, :].bitcast(F32), 0.0).then_inc(zeros_set, 1)
            pool.wait_ge(zeros_set, 1)
            nc.gpsimd.memset(ht[:, :].bitcast(F32), 0.0).then_inc(zeros_set, 1)
            pool.wait_ge(zeros_set, 2)
            nc.gpsimd.memset(ht[96:98, :].bitcast(F32), 1.0).then_inc(ones_set, 1)
            pool.wait_ge(ones_set, 1)
            pool.wait_ge(bias0_in, 16)

            def add_bias0(b, p):
                pool.wait_ge(x_in, 16 * (b + 1))
                for st in range(ST):
                    pool.wait_ge(xb_added, 2 * b + st)
                    nc.gpsimd.tensor_tensor(xy[:, p, st, :], xy[:, p, st, :], bias0[:, :], ALU.add).then_inc(xb_added, 1)

            add_bias0(0, 0)
            with pool.Fori(0, (NB - 2) // 2) as i:
                add_bias0(2 * i + 1, 1)
                add_bias0(2 * i + 2, 0)
            add_bias0(last, 1)

        @block.scalar
        def _(act):
            def copy_w0(u):
                _, g, p, h = units[u]
                act.wait_ge(unit_turned, u + 1)
                k0 = g * TG + 2 * h
                nc.scalar.activation(w0t[:, k0:k0 + 2, 2 * P * p:2 * P * (p + 1)],
                                     ps[:, unit_bank[u], :].rearrange("p (k o) -> p k o", k=2),
                                     ACT.Copy).then_inc(w0_copied, 1)

            def split_hi(u):
                act.wait_ge(unit_turned, u + 1)
                dst, src = split_views(u, 0)
                nc.scalar.activation(dst, src, ACT.Copy).then_inc(parts_hi, 1)

            def sign(b, k):
                s = arrived(act, b, ("m", k))
                nc.scalar.activation(load[:, s, :], load[:, s, :].bitcast(I32), ACT.Copy,
                                     bias=-1.0, scale=2.0).then_inc(sign_made, 1)

            def chunk_hi(b, k, first=False):
                s, _ = landed_at(b, ("m", k))
                act.wait_ge(w_made, KT * b + k + 1)
                if not (first and k < WS):
                    act.wait_ge(w_used, KT * b + k + 1 - WS)
                nc.scalar.activation(whi[:, k % WS, :], load[:, s, :], ACT.Copy).then_inc(w_hi, 1)

            def rows_hi(b, g, first=False):
                act.wait_ge(x_turned, 2 * b + g + 1)
                if not first:
                    act.wait_ge(w_used, KT * b)
                nc.scalar.activation(xhi[:, g * TG:(g + 1) * TG, :], xt[:, :, :], ACT.Copy).then_inc(x_hi, 1)

            def y_parts_hi(b, st, g):
                act.wait_ge(y_turned, 4 * b + 2 * st + g + 1)
                nc.scalar.activation(yhi[:, st, g * TG:(g + 1) * TG, :],
                                     ps[:, TR, :].rearrange("p (k m) -> p k m", k=TG), ACT.Copy).then_inc(y_hi, 1)

            def h_parts_hi(b, st):
                act.wait_ge(h_turned, 2 * b + st + 1)
                for row in (0, 64):
                    nc.scalar.activation(ht[row:row + R, st * P:(st + 1) * P],
                                         ps[0:R, SM, HT0 + st * P:HT0 + (st + 1) * P], ACT.Copy).then_inc(h_hi, 1)

            def step(b, first=False, end=False):
                if first:
                    y_parts_hi(b, 0, 0)
                    y_parts_hi(b, 0, 1)
                    for u in range(number[("b", 1)] + 1, len(units)):
                        split_hi(u)
                    h_parts_hi(b, 0)
                    rows_hi(b + 1, 0)
                    for k in range(3):
                        sign(b + 1, k)
                        chunk_hi(b + 1, k)
                        if k == 1:
                            rows_hi(b + 1, 1)
                else:
                    chunk_hi(b, 4)
                    y_parts_hi(b - 1, 1, 0)
                    chunk_hi(b, 5)
                    y_parts_hi(b - 1, 1, 1)
                    chunk_hi(b, 6)
                    if not end:
                        sign(b + 1, 0)
                    chunk_hi(b, 7)
                    if not end:
                        sign(b + 1, 1)
                        chunk_hi(b + 1, 0)
                        sign(b + 1, 2)
                    h_parts_hi(b - 1, 1)
                    if not end:
                        sign(b + 1, 3)
                        chunk_hi(b + 1, 1)
                        sign(b + 1, 4)
                        chunk_hi(b + 1, 2)
                        rows_hi(b + 1, 0)
                    y_parts_hi(b, 0, 0)
                    if not end:
                        rows_hi(b + 1, 1)
                        chunk_hi(b + 1, 3)
                    y_parts_hi(b, 0, 1)
                    if not end:
                        sign(b + 1, 5)
                    h_parts_hi(b, 0)
                if first:
                    sign(b + 1, 3)
                    chunk_hi(b + 1, 3)
                    sign(b + 1, 4)
                    sign(b + 1, 5)
                if not end:
                    sign(b + 1, 6)
                    sign(b + 1, 7)

            for u in range(8):
                copy_w0(u)
            sign(0, 0)
            rows_hi(0, 0, first=True)
            for j in range(4):
                sign(0, j + 1)
                chunk_hi(0, j, first=True)
                copy_w0(8 + 2 * j)
                copy_w0(9 + 2 * j)
                if j == 3:
                    rows_hi(0, 1, first=True)
            for j in range(4):
                if j < 3:
                    sign(0, 5 + j)
                chunk_hi(0, 4 + j, first=True)
                split_hi(W0_UNITS + 2 * j)
                split_hi(W0_UNITS + 2 * j + 1)
            s = arrived(act, 0, ("b",))
            act.wait_ge(x_lo, 2)
            nc.scalar.activation(b_sorted_view.rearrange("p (o b r) -> p o b r", o=8, b=NB),
                                 load[:, s, :].rearrange("p (b o r) -> p o b r", b=NB, o=8),
                                 ACT.Copy).then_inc(b_sorted, 1)
            for u in range(number[("a", 0)], number[("b", 1)] + 1):
                split_hi(u)
            s = arrived(act, 0, ("b1",))
            act.wait_ge(zeros_set, 1)
            for p in range(2):
                nc.scalar.activation(bt[96:97, p, :], load[96:97, s, :], ACT.Copy).then_inc(bias1_hi, 1)
            act.wait_ge(parts_stored, 32)
            act.wait_ge(ones_set, 1)
            step(0, first=True)
            with act.Fori(0, (NB - 2) // 2) as i:
                step(2 * i + 1)
                step(2 * i + 2)
            step(last, end=True)
            y_parts_hi(last, 1, 0)
            y_parts_hi(last, 1, 1)
            h_parts_hi(last, 1)

        @block.vector
        def _(dve):
            def split_lo(u):
                dve.wait_ge(parts_hi, split_count(u))
                hi, src = split_views(u, 0)
                lo, _ = split_views(u, 1)
                nc.vector.tensor_tensor(lo, src, hi.bitcast(F32), ALU.subtract).then_inc(parts_lo, 1)

            def turn_rows(b, g):
                s = arrived(dve, b, ("x", g))
                if not (isinstance(b, int) and b == 0 and g == 0):
                    dve.wait_ge(x_lo, 2 * b + g)
                nc.vector.transpose(xt[:, :, :].rearrange("p t (n q) -> p n t q", q=Q),
                                    load[:, s, :].rearrange("p (n i t) -> p n t i", t=TG, i=Q)).then_inc(x_turned, 1)

            def rows_lo(b, g):
                dve.wait_ge(x_hi, 2 * b + g + 1)
                k = slice(g * TG, (g + 1) * TG)
                nc.vector.tensor_tensor(xlo[:, k, :], xt[:, :, :], xhi[:, k, :].bitcast(F32),
                                        ALU.subtract).then_inc(x_lo, 1)

            def make_w(b, k):
                s, _ = landed_at(b, ("m", k))
                dve.wait_ge(sign_made, KT * b + k + 1)
                nc.vector.scalar_tensor_tensor(load[:, s, :], load[:, s, :], cs[:, bass.ds(b, 1)], w0t[:, k, :],
                                               ALU.mult, ALU.add).then_inc(w_made, 1)

            def chunk_lo(b, k):
                s, _ = landed_at(b, ("m", k))
                dve.wait_ge(w_hi, KT * b + k + 1)
                nc.vector.tensor_tensor(wlo[:, k % WS, :], load[:, s, :], whi[:, k % WS, :].bitcast(F32),
                                        ALU.subtract).then_inc(w_lo, 1)

            def make_y(b, p, st, oh):
                dve.wait_ge(xb_added, 2 * b + st + 1)
                if (st, oh) == (ST - 1, OH - 1):
                    dve.wait_ge(w_used, KT * (b + 1))
                else:
                    dve.wait_ge(acc_done, 3 * b + 2 * st + oh + 1)
                rows = xy[:, p, st, oh * HALF:(oh + 1) * HALF]
                nc.vector.tensor_tensor(rows, ps[:, ACC + 2 * st + oh, :], rows, ALU.add).then_inc(y_made, 1)

            def y_parts_lo(b, st, g):
                dve.wait_ge(y_hi, 4 * b + 2 * st + g + 1)
                k = slice(g * TG, (g + 1) * TG)
                nc.vector.tensor_tensor(ylo[:, st, k, :], ps[:, TR, :].rearrange("p (k m) -> p k m", k=TG),
                                        yhi[:, st, k, :].bitcast(F32), ALU.subtract).then_inc(y_lo, 1)

            def sum_h(b, st):
                dve.wait_ge(h_done, 2 * b + st + 1)
                nc.vector.tensor_reduce(hsum[:, st, :],
                                        ps[:, SM, st * 2 * R:(st + 1) * 2 * R].rearrange("p (j r) -> p r j", j=2),
                                        AX_X, ALU.add).then_inc(h_summed, 1)

            def h_parts_lo(b, st):
                dve.wait_ge(h_hi, 2 * (2 * b + st + 1))
                nc.vector.tensor_tensor(ht[32:32 + R, st * P:(st + 1) * P],
                                        ps[0:R, SM, HT0 + st * P:HT0 + (st + 1) * P],
                                        ht[0:R, st * P:(st + 1) * P].bitcast(F32), ALU.subtract).then_inc(h_lo, 1)

            def make_z(b, p, st, oh):
                dve.wait_ge(z_done, 4 * b + 2 * st + oh + 1)
                rows = xy[:, p, st, oh * HALF:(oh + 1) * HALF]
                nc.vector.tensor_tensor(rows, ps[:, ZB + oh, :], rows, ALU.add).then_inc(z_made, 1)

            def step(b, p, first=False, end=False):
                q = 1 - p
                if first:
                    y_parts_lo(b, 0, 0)
                    y_parts_lo(b, 0, 1)
                    for u in range(number[("b", 1)] + 1, len(units)):
                        split_lo(u)
                    sum_h(b, 0)
                    h_parts_lo(b, 0)
                    turn_rows(b + 1, 0)
                    rows_lo(b + 1, 0)
                    make_w(b + 1, 0)
                    chunk_lo(b + 1, 0)
                    make_w(b + 1, 1)
                    chunk_lo(b + 1, 1)
                    turn_rows(b + 1, 1)
                    rows_lo(b + 1, 1)
                    make_w(b + 1, 2)
                    chunk_lo(b + 1, 2)
                    make_z(b, p, 0, 0)
                    make_w(b + 1, 3)
                    chunk_lo(b + 1, 3)
                    make_z(b, p, 0, 1)
                    for k in range(4, 8):
                        make_w(b + 1, k)
                    return
                chunk_lo(b, 4)
                y_parts_lo(b - 1, 1, 0)
                chunk_lo(b, 5)
                y_parts_lo(b - 1, 1, 1)
                if not end:
                    turn_rows(b + 1, 0)
                chunk_lo(b, 6)
                if not end:
                    make_w(b + 1, 0)
                chunk_lo(b, 7)
                if not end:
                    make_w(b + 1, 1)
                    chunk_lo(b + 1, 0)
                sum_h(b - 1, 1)
                if not end:
                    make_w(b + 1, 2)
                h_parts_lo(b - 1, 1)
                if not end:
                    make_w(b + 1, 3)
                    chunk_lo(b + 1, 1)
                make_y(b, p, 0, 0)
                make_y(b, p, 0, 1)
                if not end:
                    chunk_lo(b + 1, 2)
                make_y(b, p, 1, 0)
                make_y(b, p, 1, 1)
                if not end:
                    rows_lo(b + 1, 0)
                    turn_rows(b + 1, 1)
                make_z(b - 1, q, 1, 0)
                y_parts_lo(b, 0, 0)
                if not end:
                    rows_lo(b + 1, 1)
                    chunk_lo(b + 1, 3)
                y_parts_lo(b, 0, 1)
                if not end:
                    make_w(b + 1, 4)
                make_z(b - 1, q, 1, 1)
                sum_h(b, 0)
                if not end:
                    make_w(b + 1, 5)
                h_parts_lo(b, 0)
                if not end:
                    make_w(b + 1, 6)
                make_z(b, p, 0, 0)
                if not end:
                    make_w(b + 1, 7)
                else:
                    y_parts_lo(b, 1, 0)
                    y_parts_lo(b, 1, 1)
                make_z(b, p, 0, 1)

            turn_rows(0, 0)
            rows_lo(0, 0)
            dve.wait_ge(coeff_in, 16)
            dve.wait_ge(w0_copied, W0_UNITS // 2)
            for j in range(4):
                make_w(0, j)
                chunk_lo(0, j)
            turn_rows(0, 1)
            rows_lo(0, 1)
            dve.wait_ge(w0_copied, W0_UNITS)
            for j in range(4):
                make_w(0, 4 + j)
                chunk_lo(0, 4 + j)
                split_lo(W0_UNITS + 2 * j)
                split_lo(W0_UNITS + 2 * j + 1)
            for u in range(number[("a", 0)], number[("b", 1)] + 1):
                split_lo(u)
            s, _ = place[("b1",)]
            dve.wait_ge(bias1_hi, 1)
            nc.vector.tensor_tensor(bias1lo[96:97, :], load[96:97, s, :], bt[96:97, 0, :].bitcast(F32),
                                    ALU.subtract).then_inc(bias1_lo, 1)
            for st in range(ST):
                for oh in range(OH):
                    make_y(0, 0, st, oh)
            step(0, 0, first=True)
            with dve.Fori(0, (NB - 2) // 2) as i:
                step(2 * i + 1, 1)
                step(2 * i + 2, 0)
            step(last, 1, end=True)
            sum_h(last, 1)
            h_parts_lo(last, 1)
            make_z(last, 1, 1, 0)
            make_z(last, 1, 1, 1)

        @block.tensor
        def _(pe):
            def turn_unit(u):
                bank = unit_bank[u]
                before = [v for v in range(u) if unit_bank[v] == bank]
                if before:
                    if before[-1] < W0_UNITS:
                        pe.wait_ge(w0_copied, before[-1] + 1)
                    else:
                        pe.wait_ge(parts_lo, split_count(before[-1]))
                unit = units[u]
                if unit[0] == "b":
                    pe.wait_ge(b_sorted, 1)
                else:
                    s = arrived(pe, 0, unit[:-1])
                if unit[0] in ("w0", "w1"):
                    h = unit[3]
                    raw = load[:, s, :].rearrange("p (t f) -> p t f", t=2)
                    for t in range(2):
                        if unit[0] == "w0":
                            src = raw[:, t, :].rearrange("p (j c) -> p c j", c=TG)
                            cut = [src[:, 2 * h + c] for c in range(2)]
                        else:
                            cut = [raw[:, t, (2 * h + c) * P:(2 * h + c + 1) * P] for c in range(2)]
                        for c in range(2):
                            at0 = c * 2 * P + t * P
                            op = nc.tensor.transpose(ps[:, bank, at0:at0 + P], cut[c], ident[:, :])
                else:
                    h = unit[1]
                    for c in range(4):
                        if unit[0] == "a":
                            src = load[:, s, (4 * h + c) * P:(4 * h + c + 1) * P]
                        else:
                            src = b_sorted_view[:, (4 * h + c) * P:(4 * h + c + 1) * P]
                        op = nc.tensor.transpose(ps[:, bank, c * P:(c + 1) * P], src, ident[:, :])
                op.then_inc(unit_turned, 1)

            def layer1(b, k, first=False):
                if k % TG == 0:
                    pe.wait_ge(x_lo, 2 * b + k // TG + 1)
                if k == 0 and not first:
                    pe.wait_ge(y_made, 4 * b)
                pe.wait_ge(w_lo, KT * b + k + 1)
                s = k % WS
                for st in range(ST):
                    rows = slice(st * P, (st + 1) * P)
                    for n, (xa, wa) in enumerate(((xhi, whi), (xhi, wlo), (xlo, whi))):
                        for oh in range(OH):
                            op = nc.tensor.matmul(ps[:, ACC + 2 * st + oh, :], xa[:, k, rows],
                                                  wa[:, s, oh * HALF:(oh + 1) * HALF],
                                                  start=(k == 0 and n == 0), stop=(k == KT - 1 and n == 2))
                            if k == KT - 1 and n == 2 and (st, oh) != (ST - 1, OH - 1):
                                op.then_inc(acc_done, 1)
                op.then_inc(w_used, 1)

            def turn_y(b, p, st, g):
                pe.wait_ge(y_made, 4 * b + 2 * st + g + 1)
                n = 4 * b + 2 * st + g
                if isinstance(n, int) and n == 0:
                    pe.wait_ge(parts_lo, split_count(number[("b", 1)]))
                else:
                    pe.wait_ge(y_lo, n)
                for c in range(TG):
                    k = g * TG + c
                    op = nc.tensor.transpose(ps[:, TR, c * P:(c + 1) * P], xy[:, p, st, k * P:(k + 1) * P], ident[:, :])
                op.then_inc(y_turned, 1)

            def adapter_h(b, p, st):
                pe.wait_ge(at_in, 16 * (b + 1))
                pe.wait_ge(y_lo, 4 * b + 2 * st + 2)
                c0 = st * 2 * R
                for k in range(KT):
                    nc.tensor.matmul(ps[:, SM, c0:c0 + 2 * R], yhi[:, st, k, :], at[:, p, k, :],
                                     start=(k == 0), stop=False, skip_group_check=True)
                    op = nc.tensor.matmul(ps[:, SM, c0:c0 + R], ylo[:, st, k, :], at[:, p, k, 0:R],
                                          start=False, stop=(k == KT - 1), skip_group_check=True)
                op.then_inc(h_done, 1)

            def turn_h(b, st):
                pe.wait_ge(h_summed, 2 * b + st + 1)
                nc.tensor.transpose(ps[0:R, SM, HT0 + st * P:HT0 + (st + 1) * P], hsum[:, st, :],
                                    ident[:, :]).then_inc(h_turned, 1)

            def layer2(b, p, st, oh, ks=range(KT), first=False):
                n = 4 * b + 2 * st + oh
                for k in ks:
                    if k == 0:
                        pe.wait_ge(y_lo, 4 * b + 2 * st + 2)
                        if not first:
                            pe.wait_ge(z_made, n - 1)
                    for i, (ya, wa) in enumerate(((yhi, w1hi), (yhi, w1lo), (ylo, w1hi))):
                        nc.tensor.matmul(ps[:, ZB + oh, :], ya[:, st, k, :], wa[:, k, oh * HALF:(oh + 1) * HALF],
                                         start=(k == 0 and i == 0), stop=False)
                if ks[-1] == KT - 1:
                    pe.wait_ge(bt_in, 48 * (b + 1))
                    pe.wait_ge(h_lo, 2 * b + st + 1)
                    nc.tensor.matmul(ps[:, ZB + oh, :], ht[:, st * P:(st + 1) * P], bt[:, p, oh * HALF:(oh + 1) * HALF],
                                     start=False, stop=True).then_inc(z_done, 1)

            def step(b, p, end=False):
                q = 1 - p
                layer1(b, 0)
                layer1(b, 1)
                turn_y(b - 1, q, 1, 0)
                layer1(b, 2)
                turn_y(b - 1, q, 1, 1)
                layer1(b, 3)
                layer1(b, 4)
                adapter_h(b - 1, q, 1)
                layer1(b, 5)
                turn_h(b - 1, 1)
                layer1(b, 6)
                layer1(b, 7)
                layer2(b - 1, q, 1, 0)
                turn_y(b, p, 0, 0)
                layer2(b - 1, q, 1, 1, range(0, 4))
                turn_y(b, p, 0, 1)
                layer2(b - 1, q, 1, 1, range(4, 8))
                adapter_h(b, p, 0)
                layer2(b, p, 0, 0, range(0, 3))
                turn_h(b, 0)
                layer2(b, p, 0, 0, range(3, 8))
                if end:
                    turn_y(b, p, 1, 0)
                    layer2(b, p, 0, 1, range(0, 4))
                    turn_y(b, p, 1, 1)
                    layer2(b, p, 0, 1, range(4, 8))
                else:
                    layer2(b, p, 0, 1)

            pe.wait_ge(ident_set, 2)
            for u in range(8):
                turn_unit(u)
            for u in (8, 9):
                turn_unit(u)
            for k in range(8):
                if k < 7:
                    turn_unit(10 + 2 * k)
                    turn_unit(11 + 2 * k)
                layer1(0, k, first=True)
            for u in range(24, number[("b", 1)] + 1):
                turn_unit(u)
            turn_y(0, 0, 0, 0)
            turn_y(0, 0, 0, 1)
            for u in range(number[("b", 1)] + 1, len(units)):
                turn_unit(u)
            adapter_h(0, 0, 0)
            pe.wait_ge(parts_lo, split_count(len(units) - 1))
            layer2(0, 0, 0, 0, range(0, 3), first=True)
            turn_h(0, 0)
            pe.wait_ge(bias1_hi, 2)
            pe.wait_ge(bias1_moved, 32)
            layer2(0, 0, 0, 0, range(3, 8), first=True)
            layer2(0, 0, 0, 1, first=True)
            with pe.Fori(0, (NB - 2) // 2) as i:
                step(2 * i + 1, 1)
                step(2 * i + 2, 0)
            step(last, 1, end=True)
            adapter_h(last, 1, 1)
            layer2(last, 1, 1, 0, range(0, 3))
            turn_h(last, 1)
            layer2(last, 1, 1, 0, range(3, 8))
            layer2(last, 1, 1, 1)


_INS = ["x", "condB_coeff", "itok_B_6_15", "mask_Bx4096x4096_ik1", "L0_cond_W", "L0_cond_b",
        "L1_cond_base_weight", "L1_cond_base_bias", "L1_cond_lora_A_w", "L1_cond_lora_B_w"]
_OUTS = [((8, 256, 1024), "float32")]


def kernel(**inputs):
    import numpy as _np
    import concourse.bacc as _bacc
    from concourse import mybir as _mybir
    from concourse.bass_utils import run_bass_kernel_spmd as _run

    nc = _bacc.Bacc("TRN2", target_bir_lowering=False, num_devices=1, dynamic_dma_scratch_size=1024)
    arrays, args = {}, []
    for name in _INS:
        a = _np.ascontiguousarray(inputs[name])
        arrays[f"in_{name}_dram"] = a
        args.append(nc.dram_tensor(f"in_{name}_dram", a.shape, _mybir.dt.from_np(a.dtype), kind="ExternalInput").ap())
    for i, (shape, dtype) in enumerate(_OUTS):
        dt = _mybir.dt.from_np(_np.dtype(dtype))
        args.append(nc.dram_tensor(f"out_{i}_dram", shape, dt, kind="ExternalOutput").ap())
    two_layer_kernel(nc, *args)
    r = _run(nc, [arrays], core_ids=[0])
    got = tuple(r.results[0][f"out_{i}_dram"] for i in range(len(_OUTS)))
    return got[0]
```

```python
from contextlib import ExitStack

import concourse.bass as bass
from concourse import mybir

F32 = mybir.dt.float32
F32R = mybir.dt.float32r
I32 = mybir.dt.int32
ALU = mybir.AluOpType
ACT = mybir.ActivationFunctionType
AX_X = mybir.AxisListType.X

P = 128
Q = 32
HALF = 512


def two_layer_kernel(nc, x, coeff, ids, mask, W0, b0, W1, b1, lora_a, lora_b, out):
    NB, S, D = x.shape
    NL, R, _ = lora_a.shape
    KT = D // P
    ST = S // P
    OH = D // HALF
    KG = D // HALF
    TG = HALF // P
    SLOTS = 5
    WS = 4
    assert (NB, S, D, R) == (8, 256, 1024, 16) and NB * R == P
    last = NB - 1

    pieces = [("x", 0), ("x", 1), ("a",), ("b",)] + [("w1", g, p) for g in range(KG) for p in range(4)]
    LEAD = len(pieces)
    batch_pieces = [("m", 0), ("m", 1), ("x", 0), ("m", 2), ("m", 3),
                    ("m", 4), ("m", 5), ("x", 1), ("m", 6), ("m", 7)]
    PER = len(batch_pieces)
    assert PER % SLOTS == 0
    WEIGHT = {"x": 64, "m": 16, "w1": 16, "a": 16 * NB, "b": 16 * NB}

    place, filled = {}, [0] * SLOTS
    for n, piece in enumerate(pieces):
        filled[n % SLOTS] += WEIGHT[piece[0]]
        place[piece] = (n % SLOTS, filled[n % SLOTS])

    def slot_of(j):
        return (LEAD + j) % SLOTS

    gain = [sum(WEIGHT[batch_pieces[j][0]] for j in range(PER) if slot_of(j) == s) for s in range(SLOTS)]

    def landed_at(b, piece):
        if isinstance(b, int) and b == 0:
            return place[piece]
        j = batch_pieces.index(piece)
        s = slot_of(j)
        upto = sum(WEIGHT[batch_pieces[i][0]] for i in range(j + 1) if slot_of(i) == s)
        return s, (b - 1) * gain[s] + filled[s] + upto

    units = [("w0", g, p, h) for g in range(KG) for p in range(4) for h in range(2)]
    units += [("a", 0), ("a", 1), ("b", 0), ("b", 1)]
    units += [("w1", g, p, h) for g in range(KG) for p in range(4) for h in range(2)]
    number = {u: n for n, u in enumerate(units)}
    LATE = number[("w1", 1, 0, 0)]
    W0_UNITS = sum(u[0] == "w0" for u in units)

    scratch_a = nc.dram_tensor("adapter_a_parts", [NB, P, KT * 2 * R], F32).ap()
    scratch_b = nc.dram_tensor("adapter_b_parts", [2, P, D], F32).ap()

    with ExitStack() as ctx:
        def sb(name, shape, dt=F32):
            return ctx.enter_context(nc.sbuf_tensor(name, shape, dt))

        def sem(name):
            return ctx.enter_context(nc.semaphore(name))

        load = sb("load", [P, SLOTS, D])
        w0t = sb("w0t", [P, KT, D])
        arena_at = nc.sbuf_base
        arena = sb("arena", [P, 2, KT, D])
        w1hi = nc.alloc_sbuf_tensor_at("w1hi", [P, KT, D], F32R, offset=arena_at)
        w1lo = nc.alloc_sbuf_tensor_at("w1lo", [P, KT, D], F32R, offset=arena_at + KT * D * 4)
        whi = sb("whi", [P, WS, D], F32R)
        wlo = sb("wlo", [P, WS, D], F32R)
        xt = sb("xt", [P, TG, S])
        xhi = sb("xhi", [P, KT, S], F32R)
        xlo = sb("xlo", [P, KT, S], F32R)
        xy = sb("xy", [P, 2, ST, D])
        yhi = sb("yhi", [P, ST, KT, P], F32R)
        ylo = sb("ylo", [P, ST, KT, P], F32R)
        bias0 = sb("bias0", [P, D])
        bias1lo = sb("bias1lo", [P, D], F32R)
        cs = sb("cs", [P, NB])
        id_row = sb("id_row", [1, NB], I32)
        ident = sb("ident", [P, P])
        at = sb("at", [P, 2, KT, 2 * R], F32R)
        bt = sb("bt", [P, 2, D], F32R)
        hsum = sb("hsum", [P, ST, R])
        ht = sb("ht", [P, S], F32R)
        a_stage = yhi[:, :, :, :].rearrange("p s k m -> p (s k m)").rearrange("p (b k r) -> p b k r", b=NB, k=KT)
        b_stage = ylo[:, :, :, :].rearrange("p s k m -> p (s k m)").rearrange("p (h o) -> p h o", h=2)

        b_sorted_view = xy[:, 1, 0, :]
        w0_raw, first_chunks = arena[:, 0], arena[:, 1]

        ps = ctx.enter_context(nc.psum_tensor("ps", [P, 8, HALF], F32))
        ACC, ZB, TR, SM = 0, 4, 6, 7
        HT0 = 128
        unit_bank = [ZB + u % 3 if u < LATE else ACC + u % 4 for u in range(len(units))]
        group, u = [], 8
        for k in range(KT):
            group.append([] if k == TG else [u, u + 1])
            u += len(group[-1])
        GROUPED = u

        landed = [sem(f"landed{s}") for s in range(SLOTS)]
        w0_in = [sem(f"w0_in{n}") for n in range(KG * 4)]
        mask_in = [sem(f"mask_in{k}") for k in range(KT)]
        b1_in = sem("b1_in")
        ids_in = sem("ids_in")
        coeff_in = sem("coeff_in")
        bias0_in = sem("bias0_in")
        x_in = sem("x_in")
        parts_stored = sem("parts_stored")
        bias1_moved = sem("bias1_moved")
        at_in = sem("at_in")
        bt_in = sem("bt_in")
        z_stored = sem("z_stored")
        ident_set = sem("ident_set")
        zeros_set = sem("zeros_set")
        ones_set = sem("ones_set")
        xb_added = sem("xb_added")
        unit_turned = sem("unit_turned")
        w0_copied = sem("w0_copied")
        parts_hi = sem("parts_hi")
        parts_lo = sem("parts_lo")
        b_sorted = sem("b_sorted")
        bias1_hi = sem("bias1_hi")
        bias1_lo = sem("bias1_lo")
        x_turned = sem("x_turned")
        x_hi = sem("x_hi")
        x_lo = sem("x_lo")
        sign_made = sem("sign_made")
        w_made = sem("w_made")
        w_hi = sem("w_hi")
        w_lo = sem("w_lo")
        w_used = sem("w_used")
        acc_done = sem("acc_done")
        y_made = sem("y_made")
        y_turned = sem("y_turned")
        y_hi = sem("y_hi")
        y_lo = sem("y_lo")
        h_done = sem("h_done")
        h_summed = sem("h_summed")
        h_turned = sem("h_turned")
        h_hi = sem("h_hi")
        h_lo = sem("h_lo")
        z_done = sem("z_done")
        z_made = sem("z_made")

        block = ctx.enter_context(nc.Block())

        def arrived(eng, b, piece):
            s, v = landed_at(b, piece)
            eng.wait_ge(landed[s], v)
            return s

        def chunk(b, k):
            if isinstance(b, int) and b == 0:
                return first_chunks[:, k, :]
            return load[:, landed_at(b, ("m", k))[0], :]

        def split_count(u):
            return u + 1 - min(u + 1, W0_UNITS)

        def split_views(u, part):
            kind = units[u][0]
            bank = ps[:, unit_bank[u], :]
            if kind == "w1":
                _, g, p, h = units[u]
                k0 = g * TG + 2 * h
                w = (w1hi, w1lo)[part]
                return w[:, k0:k0 + 2, 2 * P * p:2 * P * (p + 1)], bank.rearrange("p (k o) -> p k o", k=2)
            h = units[u][1]
            if kind == "a":
                dst = a_stage[:, :, 4 * h:4 * h + 4, part * R:(part + 1) * R].rearrange("p b k r -> p k b r")
                return dst, bank.rearrange("p (k b r) -> p k b r", k=4, b=NB)
            dst = b_stage[:, part, :].rearrange("p (m o) -> p o m", o=8)[:, 4 * h:4 * h + 4, :]
            return dst, bank.rearrange("p (o m) -> p o m", o=4)

        @block.sync
        def _(sp):
            def start_mask(dst, b, k):
                src = mask[bass.ds(b, 1)].rearrange("e (g j t) o -> (e g) t j o", g=KG, t=TG)[k // TG, k % TG]
                return sp.dma_start(dst.bitcast(I32), src)

            def start_half(dst, w, g, p):
                src = w[2 * P * p:2 * P * (p + 1), g * HALF:(g + 1) * HALF].rearrange("(t q) f -> q t f", q=P)
                return sp.dma_start(dst.rearrange("p (t f) -> p t f", t=2), src)

            def start(s, b, piece):
                kind = piece[0]
                if kind == "x":
                    for a in range(4):
                        c0 = piece[1] * HALF + a * P
                        src = x[bass.ds(b, 1), :, c0:c0 + P].rearrange("e (n q) f -> (e q) n f", q=Q)
                        dst = load[a * Q:(a + 1) * Q, s, :].rearrange("q (n f) -> q n f", f=P)
                        sp.dma_start(dst, src).then_inc(landed[s], 16)
                elif kind == "m":
                    start_mask(load[:, s, :], b, piece[1]).then_inc(landed[s], 16)
                else:
                    start_half(load[:, s, :], W1, piece[1], piece[2]).then_inc(landed[s], 16)

            def start_adapter(e):
                name = sp.value_load(id_row[0:1, e:e + 1], min_val=0, max_val=NL - 1)
                s, _ = place[("a",)]
                src = lora_a[bass.ds(name, 1)].rearrange("e r d -> (e r) d")
                sp.dma_start(load[e * R:(e + 1) * R, s, :], src).then_inc(landed[s], 16)
                s, _ = place[("b",)]
                src = lora_b[bass.ds(name, 1)].rearrange("e (p o) r -> (e p) (o r)", p=P)
                sp.dma_start(load[:, s, e * P:(e + 1) * P], src).then_inc(landed[s], 16)

            def slot_free(b, piece):
                kind = piece[0]
                if kind == "x":
                    sp.wait_ge(x_turned, 2 * b + piece[1] + 1)
                elif kind == "m":
                    sp.wait_ge(w_lo, KT * b + piece[1] + 1)
                elif kind == "b":
                    sp.wait_ge(b_sorted, 1)
                else:
                    sp.wait_ge(unit_turned, number[(*piece, 1)] + 1)

            def start_batch_piece(b, j, first):
                if j >= SLOTS:
                    slot_free(b, batch_pieces[j - SLOTS])
                elif first:
                    slot_free(0, pieces[LEAD + j - SLOTS])
                else:
                    slot_free(b - 1, batch_pieces[PER + j - SLOTS])
                start(slot_of(j), b, batch_pieces[j])

            def load_rows(b, p, wait):
                if wait:
                    sp.wait_ge(z_stored, 64 * (b - 1))
                elif b == 1:
                    sp.wait_ge(unit_turned, number[("b", 1)] + 1)
                src = x[bass.ds(b, 1)].rearrange("e (t q) d -> (e q) t d", q=P)
                sp.dma_start(xy[:, p], src).then_inc(x_in, 16)

            def load_adapter(b, p, wait):
                if wait:
                    sp.wait_ge(z_done, 4 * (b - 1))
                src = scratch_a[bass.ds(b, 1)].rearrange("e p f -> (e p) f")
                sp.dma_start(at[:, p].rearrange("p k r -> p (k r)").bitcast(F32), src).then_inc(at_in, 16)
                for row, part in ((0, 0), (32, 0), (64, 1)):
                    src = scratch_b[part, bass.ds(b * R, R), :]
                    sp.dma_start(bt[row:row + R, p, :].bitcast(F32), src).then_inc(bt_in, 16)

            def store_z(b, p, st, oh):
                sp.wait_ge(z_made, 4 * b + 2 * st + oh + 1)
                dst = out[bass.ds(b, 1), st * P:(st + 1) * P, oh * HALF:(oh + 1) * HALF].rearrange("e q o -> (e q) o")
                sp.dma_start(dst, xy[:, p, st, oh * HALF:(oh + 1) * HALF]).then_inc(z_stored, 16)

            def step(b, p, first=False, end=False):
                q = 1 - p
                if not end:
                    for j in (0, 1, 2, 3, 4, 7, 5, 6, 8) if first else (2, 0, 1, 3, 7, 4, 5, 6, 8):
                        start_batch_piece(b + 1, j, first)
                if not first:
                    store_z(b - 1, q, 1, 0)
                if not end:
                    start_batch_piece(b + 1, 9, first)
                if not first:
                    store_z(b - 1, q, 1, 1)
                if not end:
                    load_rows(b + 1, q, not first)
                    load_adapter(b + 1, q, not first)
                store_z(b, p, 0, 0)
                store_z(b, p, 0, 1)

            sp.dma_start(id_row[:, :], ids.rearrange("(e b) -> e b", e=1)).then_inc(ids_in, 16)
            def start_w0(g, p):
                n = 4 * g + p
                start_half(w0_raw[:, n, :], W0, g, p).then_inc(w0_in[n], 16)

            def start_first_mask(k):
                start_mask(first_chunks[:, k, :], 0, k).then_inc(mask_in[k], 16)

            def start_w1(g, p):
                piece = ("w1", g, p)
                n = pieces.index(piece)
                if n >= SLOTS:
                    slot_free(0, pieces[n - SLOTS])
                start(n % SLOTS, 0, piece)

            for p in range(4):
                start_w0(0, p)
            start(0, 0, ("x", 0))
            start_first_mask(0)
            sp.dma_start(cs[:, :], coeff.rearrange("(e b) -> e b", e=1).to_broadcast([P, NB])).then_inc(coeff_in, 16)
            start_first_mask(1)
            start_w0(1, 0)
            start_first_mask(2)
            start_w0(1, 1)
            start_first_mask(3)
            start_w0(1, 2)
            start(1, 0, ("x", 1))
            start_w0(1, 3)
            sp.wait_ge(ids_in, 16)
            for k in range(4):
                start_first_mask(4 + k)
                start_adapter(2 * k)
                start_adapter(2 * k + 1)
            start_w1(0, 0)
            start_w1(0, 1)
            sp.dma_start(bias1lo[96:97, :].bitcast(F32), b1.rearrange("(e o) -> e o", e=1)).then_inc(b1_in, 16)
            sp.dma_start(bias0[:, :], b0.rearrange("(e o) -> e o", e=1).to_broadcast([P, D])).then_inc(bias0_in, 16)
            load_rows(0, 0, False)
            start_w1(0, 2)
            start_w1(0, 3)
            start_w1(1, 0)
            sp.wait_ge(parts_lo, split_count(number[("b", 1)]))
            sp.dma_start(scratch_a.rearrange("b p f -> p b f"), a_stage.rearrange("p b k r -> p b (k r)").bitcast(F32)).then_inc(parts_stored, 16)
            sp.dma_start(scratch_b.rearrange("h p o -> p h o"), b_stage.bitcast(F32)).then_inc(parts_stored, 16)
            for p in range(1, 4):
                start_w1(1, p)
            sp.wait_ge(bias1_lo, 1)
            sp.wait_ge(zeros_set, 1)
            for p in range(2):
                sp.dma_start(bt[97:98, p, :].bitcast(F32), bias1lo[96:97, :].bitcast(F32)).then_inc(bias1_moved, 16)
            sp.wait_ge(parts_stored, 32)
            load_adapter(0, 0, False)
            step(0, 0, first=True)
            with sp.Fori(0, (NB - 2) // 2) as i:
                step(2 * i + 1, 1)
                step(2 * i + 2, 0)
            step(last, 1, end=True)
            store_z(last, 1, 1, 0)
            store_z(last, 1, 1, 1)
            sp.wait_ge(z_stored, 64 * NB)

        @block.gpsimd
        def _(pool):
            nc.gpsimd.memset(ident[:, :], 0.0).then_inc(ident_set, 1)
            pool.wait_ge(ident_set, 1)
            nc.gpsimd.affine_select(out=ident[:, :], in_=ident[:, :], compare_op=ALU.not_equal, fill=1.0, base=0,
                                    pattern=[[-1, P]], channel_multiplier=1).then_inc(ident_set, 1)
            pool.wait_ge(ident_set, 2)
            nc.gpsimd.memset(bt[:, :, :].bitcast(F32), 0.0).then_inc(zeros_set, 1)
            pool.wait_ge(zeros_set, 1)
            nc.gpsimd.memset(ht[:, :].bitcast(F32), 0.0).then_inc(zeros_set, 1)
            pool.wait_ge(zeros_set, 2)
            nc.gpsimd.memset(ht[96:98, :].bitcast(F32), 1.0).then_inc(ones_set, 1)
            pool.wait_ge(ones_set, 1)
            pool.wait_ge(bias0_in, 16)

            def add_bias0(b, p):
                pool.wait_ge(x_in, 16 * (b + 1))
                for st in range(ST):
                    pool.wait_ge(xb_added, 2 * b + st)
                    nc.gpsimd.tensor_tensor(xy[:, p, st, :], xy[:, p, st, :], bias0[:, :], ALU.add).then_inc(xb_added, 1)

            add_bias0(0, 0)
            with pool.Fori(0, (NB - 2) // 2) as i:
                add_bias0(2 * i + 1, 1)
                add_bias0(2 * i + 2, 0)
            add_bias0(last, 1)

        @block.scalar
        def _(act):
            def copy_w0(u):
                _, g, p, h = units[u]
                act.wait_ge(unit_turned, u + 1)
                k0 = g * TG + 2 * h
                nc.scalar.activation(w0t[:, k0:k0 + 2, 2 * P * p:2 * P * (p + 1)],
                                     ps[:, unit_bank[u], :].rearrange("p (k o) -> p k o", k=2),
                                     ACT.Copy).then_inc(w0_copied, 1)

            def split_hi(u):
                act.wait_ge(unit_turned, u + 1)
                dst, src = split_views(u, 0)
                nc.scalar.activation(dst, src, ACT.Copy).then_inc(parts_hi, 1)

            def sign(b, k):
                if isinstance(b, int) and b == 0:
                    act.wait_ge(mask_in[k], 16)
                else:
                    arrived(act, b, ("m", k))
                nc.scalar.activation(chunk(b, k), chunk(b, k).bitcast(I32), ACT.Copy,
                                     bias=-1.0, scale=2.0).then_inc(sign_made, 1)

            def chunk_hi(b, k, first=False):
                act.wait_ge(w_made, KT * b + k + 1)
                if not (first and k < WS):
                    act.wait_ge(w_used, KT * b + k + 1 - WS)
                nc.scalar.activation(whi[:, k % WS, :], chunk(b, k), ACT.Copy).then_inc(w_hi, 1)

            def rows_hi(b, g, first=False):
                act.wait_ge(x_turned, 2 * b + g + 1)
                if not first:
                    act.wait_ge(w_used, KT * b)
                nc.scalar.activation(xhi[:, g * TG:(g + 1) * TG, :], xt[:, :, :], ACT.Copy).then_inc(x_hi, 1)

            def y_parts_hi(b, st, g):
                act.wait_ge(y_turned, 4 * b + 2 * st + g + 1)
                nc.scalar.activation(yhi[:, st, g * TG:(g + 1) * TG, :],
                                     ps[:, TR, :].rearrange("p (k m) -> p k m", k=TG), ACT.Copy).then_inc(y_hi, 1)

            def h_parts_hi(b, st):
                act.wait_ge(h_turned, 2 * b + st + 1)
                for row in (0, 64):
                    nc.scalar.activation(ht[row:row + R, st * P:(st + 1) * P],
                                         ps[0:R, SM, HT0 + st * P:HT0 + (st + 1) * P], ACT.Copy).then_inc(h_hi, 1)

            def step(b, first=False, end=False):
                if first:
                    y_parts_hi(b, 0, 0)
                    for u in range(LATE, LATE + 4):
                        split_hi(u)
                    y_parts_hi(b, 0, 1)
                    for u in range(LATE + 4, len(units)):
                        split_hi(u)
                    sign(b + 1, 0)
                    rows_hi(b + 1, 0)
                    sign(b + 1, 1)
                    h_parts_hi(b, 0)
                    chunk_hi(b + 1, 0)
                    sign(b + 1, 2)
                    chunk_hi(b + 1, 1)
                    sign(b + 1, 3)
                    rows_hi(b + 1, 1)
                    chunk_hi(b + 1, 2)
                    sign(b + 1, 4)
                    chunk_hi(b + 1, 3)
                else:
                    chunk_hi(b, 4)
                    y_parts_hi(b - 1, 1, 0)
                    chunk_hi(b, 5)
                    y_parts_hi(b - 1, 1, 1)
                    chunk_hi(b, 6)
                    if not end:
                        sign(b + 1, 0)
                    chunk_hi(b, 7)
                    if not end:
                        sign(b + 1, 1)
                        chunk_hi(b + 1, 0)
                        sign(b + 1, 2)
                    h_parts_hi(b - 1, 1)
                    if not end:
                        sign(b + 1, 3)
                        chunk_hi(b + 1, 1)
                        sign(b + 1, 4)
                        chunk_hi(b + 1, 2)
                        rows_hi(b + 1, 0)
                    y_parts_hi(b, 0, 0)
                    if not end:
                        rows_hi(b + 1, 1)
                        chunk_hi(b + 1, 3)
                    y_parts_hi(b, 0, 1)
                    if not end:
                        sign(b + 1, 5)
                    h_parts_hi(b, 0)
                if first:
                    sign(b + 1, 5)
                if not end:
                    sign(b + 1, 6)
                    sign(b + 1, 7)

            for u in range(8):
                copy_w0(u)
            rows_hi(0, 0, first=True)
            sign(0, 0)
            sign(0, 1)
            for k in range(KT):
                chunk_hi(0, k, first=True)
                if k == 2:
                    rows_hi(0, 1, first=True)
                for u in group[k]:
                    if u < W0_UNITS:
                        copy_w0(u)
                    else:
                        split_hi(u)
                if k == 4:
                    s = arrived(act, 0, ("b",))
                    nc.scalar.activation(b_sorted_view.rearrange("p (o b r) -> p o b r", o=8, b=NB),
                                         load[:, s, :].rearrange("p (b o r) -> p o b r", b=NB, o=8),
                                         ACT.Copy).then_inc(b_sorted, 1)
                if k < KT - 2:
                    sign(0, k + 2)
            act.wait_ge(b1_in, 16)
            act.wait_ge(zeros_set, 1)
            for p in range(2):
                nc.scalar.activation(bt[96:97, p, :], bias1lo[96:97, :].bitcast(F32), ACT.Copy).then_inc(bias1_hi, 1)
            for u in range(GROUPED, LATE):
                split_hi(u)
            act.wait_ge(parts_stored, 32)
            act.wait_ge(ones_set, 1)
            step(0, first=True)
            with act.Fori(0, (NB - 2) // 2) as i:
                step(2 * i + 1)
                step(2 * i + 2)
            step(last, end=True)
            y_parts_hi(last, 1, 0)
            y_parts_hi(last, 1, 1)
            h_parts_hi(last, 1)

        @block.vector
        def _(dve):
            def split_lo(u):
                dve.wait_ge(parts_hi, split_count(u))
                hi, src = split_views(u, 0)
                lo, _ = split_views(u, 1)
                nc.vector.tensor_tensor(lo, src, hi.bitcast(F32), ALU.subtract).then_inc(parts_lo, 1)

            def turn_rows(b, g):
                s = arrived(dve, b, ("x", g))
                if not (isinstance(b, int) and b == 0 and g == 0):
                    dve.wait_ge(x_lo, 2 * b + g)
                nc.vector.transpose(xt[:, :, :].rearrange("p t (n q) -> p n t q", q=Q),
                                    load[:, s, :].rearrange("p (n i t) -> p n t i", t=TG, i=Q)).then_inc(x_turned, 1)

            def rows_lo(b, g):
                dve.wait_ge(x_hi, 2 * b + g + 1)
                k = slice(g * TG, (g + 1) * TG)
                nc.vector.tensor_tensor(xlo[:, k, :], xt[:, :, :], xhi[:, k, :].bitcast(F32),
                                        ALU.subtract).then_inc(x_lo, 1)

            def make_w(b, k):
                dve.wait_ge(sign_made, KT * b + k + 1)
                nc.vector.scalar_tensor_tensor(chunk(b, k), chunk(b, k), cs[:, bass.ds(b, 1)], w0t[:, k, :],
                                               ALU.mult, ALU.add).then_inc(w_made, 1)

            def chunk_lo(b, k):
                dve.wait_ge(w_hi, KT * b + k + 1)
                nc.vector.tensor_tensor(wlo[:, k % WS, :], chunk(b, k), whi[:, k % WS, :].bitcast(F32),
                                        ALU.subtract).then_inc(w_lo, 1)

            def make_y(b, p, st, oh):
                dve.wait_ge(xb_added, 2 * b + st + 1)
                if (st, oh) == (ST - 1, OH - 1):
                    dve.wait_ge(w_used, KT * (b + 1))
                else:
                    dve.wait_ge(acc_done, 3 * b + 2 * st + oh + 1)
                rows = xy[:, p, st, oh * HALF:(oh + 1) * HALF]
                nc.vector.tensor_tensor(rows, ps[:, ACC + 2 * st + oh, :], rows, ALU.add).then_inc(y_made, 1)

            def y_parts_lo(b, st, g):
                dve.wait_ge(y_hi, 4 * b + 2 * st + g + 1)
                k = slice(g * TG, (g + 1) * TG)
                nc.vector.tensor_tensor(ylo[:, st, k, :], ps[:, TR, :].rearrange("p (k m) -> p k m", k=TG),
                                        yhi[:, st, k, :].bitcast(F32), ALU.subtract).then_inc(y_lo, 1)

            def sum_h(b, st):
                dve.wait_ge(h_done, 2 * b + st + 1)
                nc.vector.tensor_reduce(hsum[:, st, :],
                                        ps[:, SM, st * 2 * R:(st + 1) * 2 * R].rearrange("p (j r) -> p r j", j=2),
                                        AX_X, ALU.add).then_inc(h_summed, 1)

            def h_parts_lo(b, st):
                dve.wait_ge(h_hi, 2 * (2 * b + st + 1))
                nc.vector.tensor_tensor(ht[32:32 + R, st * P:(st + 1) * P],
                                        ps[0:R, SM, HT0 + st * P:HT0 + (st + 1) * P],
                                        ht[0:R, st * P:(st + 1) * P].bitcast(F32), ALU.subtract).then_inc(h_lo, 1)

            def make_z(b, p, st, oh):
                dve.wait_ge(z_done, 4 * b + 2 * st + oh + 1)
                rows = xy[:, p, st, oh * HALF:(oh + 1) * HALF]
                nc.vector.tensor_tensor(rows, ps[:, ZB + oh, :], rows, ALU.add).then_inc(z_made, 1)

            def step(b, p, first=False, end=False):
                q = 1 - p
                if first:
                    y_parts_lo(b, 0, 0)
                    for u in range(LATE, LATE + 4):
                        split_lo(u)
                    y_parts_lo(b, 0, 1)
                    for u in range(LATE + 4, len(units)):
                        split_lo(u)
                    turn_rows(b + 1, 0)
                    sum_h(b, 0)
                    make_w(b + 1, 0)
                    rows_lo(b + 1, 0)
                    make_w(b + 1, 1)
                    h_parts_lo(b, 0)
                    chunk_lo(b + 1, 0)
                    make_w(b + 1, 2)
                    chunk_lo(b + 1, 1)
                    turn_rows(b + 1, 1)
                    make_w(b + 1, 3)
                    chunk_lo(b + 1, 2)
                    make_z(b, p, 0, 0)
                    chunk_lo(b + 1, 3)
                    rows_lo(b + 1, 1)
                    make_z(b, p, 0, 1)
                    for k in range(4, 8):
                        make_w(b + 1, k)
                    return
                chunk_lo(b, 4)
                y_parts_lo(b - 1, 1, 0)
                chunk_lo(b, 5)
                y_parts_lo(b - 1, 1, 1)
                if not end:
                    turn_rows(b + 1, 0)
                chunk_lo(b, 6)
                if not end:
                    make_w(b + 1, 0)
                chunk_lo(b, 7)
                if not end:
                    make_w(b + 1, 1)
                    chunk_lo(b + 1, 0)
                sum_h(b - 1, 1)
                if not end:
                    make_w(b + 1, 2)
                h_parts_lo(b - 1, 1)
                if not end:
                    make_w(b + 1, 3)
                    chunk_lo(b + 1, 1)
                make_y(b, p, 0, 0)
                make_y(b, p, 0, 1)
                if not end:
                    chunk_lo(b + 1, 2)
                make_y(b, p, 1, 0)
                make_y(b, p, 1, 1)
                if not end:
                    rows_lo(b + 1, 0)
                    turn_rows(b + 1, 1)
                make_z(b - 1, q, 1, 0)
                y_parts_lo(b, 0, 0)
                if not end:
                    rows_lo(b + 1, 1)
                    chunk_lo(b + 1, 3)
                y_parts_lo(b, 0, 1)
                if not end:
                    make_w(b + 1, 4)
                make_z(b - 1, q, 1, 1)
                sum_h(b, 0)
                if not end:
                    make_w(b + 1, 5)
                h_parts_lo(b, 0)
                if not end:
                    make_w(b + 1, 6)
                make_z(b, p, 0, 0)
                if not end:
                    make_w(b + 1, 7)
                else:
                    y_parts_lo(b, 1, 0)
                    y_parts_lo(b, 1, 1)
                make_z(b, p, 0, 1)

            turn_rows(0, 0)
            rows_lo(0, 0)
            dve.wait_ge(coeff_in, 16)
            dve.wait_ge(w0_copied, W0_UNITS // 2)
            make_w(0, 0)
            for k in range(KT):
                if k == 3:
                    rows_lo(0, 1)
                    chunk_lo(0, 3)
                    dve.wait_ge(w0_copied, W0_UNITS)
                    make_w(0, 4)
                else:
                    if k < KT - 1:
                        make_w(0, k + 1)
                    chunk_lo(0, k)
                if k == 1:
                    turn_rows(0, 1)
                for u in group[k]:
                    if u >= W0_UNITS:
                        split_lo(u)
            dve.wait_ge(bias1_hi, 2)
            nc.vector.tensor_tensor(bias1lo[96:97, :], bias1lo[96:97, :].bitcast(F32), bt[96:97, 0, :].bitcast(F32),
                                    ALU.subtract).then_inc(bias1_lo, 1)
            make_y(0, 0, 0, 0)
            make_y(0, 0, 0, 1)
            for u in range(GROUPED, LATE):
                split_lo(u)
            make_y(0, 0, 1, 0)
            make_y(0, 0, 1, 1)
            step(0, 0, first=True)
            with dve.Fori(0, (NB - 2) // 2) as i:
                step(2 * i + 1, 1)
                step(2 * i + 2, 0)
            step(last, 1, end=True)
            sum_h(last, 1)
            h_parts_lo(last, 1)
            make_z(last, 1, 1, 0)
            make_z(last, 1, 1, 1)

        @block.tensor
        def _(pe):
            def turn_unit(u):
                bank = unit_bank[u]
                before = [v for v in range(u) if unit_bank[v] == bank]
                if u >= LATE and not before:
                    pe.wait_ge(y_made, 4)
                if before:
                    if before[-1] < W0_UNITS:
                        pe.wait_ge(w0_copied, before[-1] + 1)
                    else:
                        pe.wait_ge(parts_lo, split_count(before[-1]))
                unit = units[u]
                if unit[0] == "b":
                    pe.wait_ge(b_sorted, 1)
                elif unit[0] == "w0":
                    pe.wait_ge(w0_in[4 * unit[1] + unit[2]], 16)
                else:
                    s = arrived(pe, 0, unit[:-1])
                if unit[0] in ("w0", "w1"):
                    h = unit[3]
                    raw = w0_raw[:, 4 * unit[1] + unit[2], :] if unit[0] == "w0" else load[:, s, :]
                    raw = raw.rearrange("p (t f) -> p t f", t=2)
                    for t in range(2):
                        if unit[0] == "w0":
                            src = raw[:, t, :].rearrange("p (j c) -> p c j", c=TG)
                            cut = [src[:, 2 * h + c] for c in range(2)]
                        else:
                            cut = [raw[:, t, (2 * h + c) * P:(2 * h + c + 1) * P] for c in range(2)]
                        for c in range(2):
                            at0 = c * 2 * P + t * P
                            op = nc.tensor.transpose(ps[:, bank, at0:at0 + P], cut[c], ident[:, :])
                else:
                    h = unit[1]
                    for c in range(4):
                        if unit[0] == "a":
                            src = load[:, s, (4 * h + c) * P:(4 * h + c + 1) * P]
                        else:
                            src = b_sorted_view[:, (4 * h + c) * P:(4 * h + c + 1) * P]
                        op = nc.tensor.transpose(ps[:, bank, c * P:(c + 1) * P], src, ident[:, :])
                op.then_inc(unit_turned, 1)

            def layer1(b, k, first=False):
                if k % TG == 0:
                    pe.wait_ge(x_lo, 2 * b + k // TG + 1)
                if k == 0 and not first:
                    pe.wait_ge(y_made, 4 * b)
                pe.wait_ge(w_lo, KT * b + k + 1)
                s = k % WS
                for st in range(ST):
                    rows = slice(st * P, (st + 1) * P)
                    for n, (xa, wa) in enumerate(((xhi, whi), (xhi, wlo), (xlo, whi))):
                        for oh in range(OH):
                            op = nc.tensor.matmul(ps[:, ACC + 2 * st + oh, :], xa[:, k, rows],
                                                  wa[:, s, oh * HALF:(oh + 1) * HALF],
                                                  start=(k == 0 and n == 0), stop=(k == KT - 1 and n == 2))
                            if k == KT - 1 and n == 2 and (st, oh) != (ST - 1, OH - 1):
                                op.then_inc(acc_done, 1)
                op.then_inc(w_used, 1)

            def turn_y(b, p, st, g):
                pe.wait_ge(y_made, 4 * b + 2 * st + g + 1)
                n = 4 * b + 2 * st + g
                if isinstance(n, int) and n == 0:
                    pe.wait_ge(parts_lo, split_count(max(u for u in range(LATE) if unit_bank[u] == TR)))
                else:
                    pe.wait_ge(y_lo, n)
                for c in range(TG):
                    k = g * TG + c
                    op = nc.tensor.transpose(ps[:, TR, c * P:(c + 1) * P], xy[:, p, st, k * P:(k + 1) * P], ident[:, :])
                op.then_inc(y_turned, 1)

            def adapter_h(b, p, st):
                pe.wait_ge(at_in, 16 * (b + 1))
                pe.wait_ge(y_lo, 4 * b + 2 * st + 2)
                c0 = st * 2 * R
                for k in range(KT):
                    nc.tensor.matmul(ps[:, SM, c0:c0 + 2 * R], yhi[:, st, k, :], at[:, p, k, :],
                                     start=(k == 0), stop=False, skip_group_check=True)
                    op = nc.tensor.matmul(ps[:, SM, c0:c0 + R], ylo[:, st, k, :], at[:, p, k, 0:R],
                                          start=False, stop=(k == KT - 1), skip_group_check=True)
                op.then_inc(h_done, 1)

            def turn_h(b, st):
                pe.wait_ge(h_summed, 2 * b + st + 1)
                nc.tensor.transpose(ps[0:R, SM, HT0 + st * P:HT0 + (st + 1) * P], hsum[:, st, :],
                                    ident[:, :]).then_inc(h_turned, 1)

            def layer2(b, p, st, oh, ks=range(KT), first=False):
                n = 4 * b + 2 * st + oh
                for k in ks:
                    if k == 0:
                        pe.wait_ge(y_lo, 4 * b + 2 * st + 2)
                        if not first:
                            pe.wait_ge(z_made, n - 1)
                    for i, (ya, wa) in enumerate(((yhi, w1hi), (yhi, w1lo), (ylo, w1hi))):
                        nc.tensor.matmul(ps[:, ZB + oh, :], ya[:, st, k, :], wa[:, k, oh * HALF:(oh + 1) * HALF],
                                         start=(k == 0 and i == 0), stop=False)
                if ks[-1] == KT - 1:
                    pe.wait_ge(bt_in, 48 * (b + 1))
                    pe.wait_ge(h_lo, 2 * b + st + 1)
                    nc.tensor.matmul(ps[:, ZB + oh, :], ht[:, st * P:(st + 1) * P], bt[:, p, oh * HALF:(oh + 1) * HALF],
                                     start=False, stop=True).then_inc(z_done, 1)

            def step(b, p, end=False):
                q = 1 - p
                layer1(b, 0)
                layer1(b, 1)
                turn_y(b - 1, q, 1, 0)
                layer1(b, 2)
                turn_y(b - 1, q, 1, 1)
                layer1(b, 3)
                layer1(b, 4)
                adapter_h(b - 1, q, 1)
                layer1(b, 5)
                turn_h(b - 1, 1)
                layer1(b, 6)
                layer1(b, 7)
                layer2(b - 1, q, 1, 0)
                turn_y(b, p, 0, 0)
                layer2(b - 1, q, 1, 1, range(0, 4))
                turn_y(b, p, 0, 1)
                layer2(b - 1, q, 1, 1, range(4, 8))
                adapter_h(b, p, 0)
                layer2(b, p, 0, 0, range(0, 3))
                turn_h(b, 0)
                layer2(b, p, 0, 0, range(3, 8))
                if end:
                    turn_y(b, p, 1, 0)
                    layer2(b, p, 0, 1, range(0, 4))
                    turn_y(b, p, 1, 1)
                    layer2(b, p, 0, 1, range(4, 8))
                else:
                    layer2(b, p, 0, 1)

            pe.wait_ge(ident_set, 2)
            for u in range(8):
                turn_unit(u)
            for u in group[0]:
                turn_unit(u)
            for k in range(KT):
                for u in group[k + 1] if k < KT - 1 else ():
                    turn_unit(u)
                layer1(0, k, first=True)
            for u in range(GROUPED, LATE):
                turn_unit(u)
            turn_y(0, 0, 0, 0)
            for u in range(LATE, LATE + 4):
                turn_unit(u)
            turn_y(0, 0, 0, 1)
            for u in range(LATE + 4, len(units)):
                turn_unit(u)
            adapter_h(0, 0, 0)
            pe.wait_ge(parts_lo, split_count(len(units) - 1))
            layer2(0, 0, 0, 0, range(0, 3), first=True)
            turn_h(0, 0)
            pe.wait_ge(bias1_hi, 2)
            pe.wait_ge(bias1_moved, 32)
            layer2(0, 0, 0, 0, range(3, 8), first=True)
            layer2(0, 0, 0, 1, first=True)
            with pe.Fori(0, (NB - 2) // 2) as i:
                step(2 * i + 1, 1)
                step(2 * i + 2, 0)
            step(last, 1, end=True)
            adapter_h(last, 1, 1)
            layer2(last, 1, 1, 0, range(0, 3))
            turn_h(last, 1)
            layer2(last, 1, 1, 0, range(3, 8))
            layer2(last, 1, 1, 1)


_INS = ["x", "condB_coeff", "itok_B_6_15", "mask_Bx4096x4096_ik1", "L0_cond_W", "L0_cond_b",
        "L1_cond_base_weight", "L1_cond_base_bias", "L1_cond_lora_A_w", "L1_cond_lora_B_w"]
_OUTS = [((8, 256, 1024), "float32")]


def kernel(**inputs):
    import numpy as _np
    import concourse.bacc as _bacc
    from concourse import mybir as _mybir
    from concourse.bass_utils import run_bass_kernel_spmd as _run

    nc = _bacc.Bacc("TRN2", target_bir_lowering=False, num_devices=1, dynamic_dma_scratch_size=1024)
    arrays, args = {}, []
    for name in _INS:
        a = _np.ascontiguousarray(inputs[name])
        arrays[f"in_{name}_dram"] = a
        args.append(nc.dram_tensor(f"in_{name}_dram", a.shape, _mybir.dt.from_np(a.dtype), kind="ExternalInput").ap())
    for i, (shape, dtype) in enumerate(_OUTS):
        dt = _mybir.dt.from_np(_np.dtype(dtype))
        args.append(nc.dram_tensor(f"out_{i}_dram", shape, dt, kind="ExternalOutput").ap())
    two_layer_kernel(nc, *args)
    r = _run(nc, [arrays], core_ids=[0])
    got = tuple(r.results[0][f"out_{i}_dram"] for i in range(len(_OUTS)))
    return got[0]
```
